# Optimizing a Trainium2 kernel written in Bass

```python
import numpy as np
import jax
import jax.numpy as jnp

def _softmax(x, axis=-1):
    return jax.nn.softmax(x, axis=axis)

def _gelu(x):
    return jax.nn.gelu(x, approximate=True)

def _silu(x):
    return jax.nn.silu(x)

def _sigmoid(x):
    return jax.nn.sigmoid(x)

def _layernorm(x, axis=-1, eps=1e-05):
    m = jnp.mean(x, axis=axis, keepdims=True)
    v = jnp.var(x, axis=axis, keepdims=True)
    return (x - m) / jnp.sqrt(v + eps)

def _scatter_add(tgt, idx, src, axis=0):
    return tgt.at[idx].add(src)

def _segment_sum(src, seg, n):
    return jax.ops.segment_sum(src, seg, n)
kernel_name = 'mk_cond_seq_d2_seqx_r2_ed7e4c'

def setup_inputs(seed: int=0):
    np.random.seed(seed)
    _w = jnp.asarray

    def _rec_inputs():
        import jax
        import jax.numpy as jnp
        _rk = jax.random.key(seed)
        x = -1.528e-05 + 0.9999 * jax.random.normal(jax.random.fold_in(_rk, 1), (128, 128, 1024), jnp.float32)
        _lenS = 128 - jax.random.randint(jax.random.fold_in(_rk, 7), (128,), 0, max(1, 128 // 4) + 1, jnp.int32)
        _lenS2 = 128 - jax.random.randint(jax.random.fold_in(_rk, 8), (128,), 0, max(1, 128 // 4) + 1, jnp.int32)
        itok_B_1_2 = jax.random.randint(jax.random.fold_in(_rk, 11), (128,), 1, 3, jnp.int32)
        return (x, itok_B_1_2)
    x, itok_B_1_2 = _rec_inputs()

    def _L0_cond_setup():
        import jax, jax.numpy as jnp
        import numpy as np
        H = 1024
        K = 512
        R = 3
        B = 8
        S = 1024
        LN_EPS = 1e-05
        key = jax.random.key(seed)
        ks = jax.random.split(key, 8)
        sd_d = 1.0 / np.sqrt(H)
        sd_u = 1.0 / np.sqrt(K)
        return {'role': jax.random.randint(ks[0], (B,), 0, R), 'hidden_states': jax.random.normal(ks[1], (B, S, H), dtype=jnp.float32), 'W_down': jax.random.uniform(ks[2], (R, H, K), jnp.float32, -sd_d, sd_d), 'b_down': jax.random.uniform(ks[3], (R, K), jnp.float32, -sd_d, sd_d), 'W_up': jax.random.uniform(ks[4], (R, K, H), jnp.float32, -sd_u, sd_u), 'b_up': jax.random.uniform(ks[5], (R, H), jnp.float32, -sd_u, sd_u), 'gamma': jnp.ones((R, H), jnp.float32), 'beta': jnp.zeros((R, H), jnp.float32)}
    _L0_cond_all = _L0_cond_setup()
    _L0_cond_in = {k: v for k, v in _L0_cond_all.items() if k in ('W_down', 'b_down', 'W_up', 'b_up', 'gamma', 'beta')}
    del _L0_cond_all

    def _L1_cond_setup():
        import jax, jax.numpy as jnp
        import numpy as np
        B, S, H = (8, 1024, 1024)
        BN = 512
        E = 3
        LN_EPS = 1e-05
        key = jax.random.key(seed)
        ks = jax.random.split(key, 8)
        stream = jax.random.randint(ks[0], (B,), 0, E, dtype=jnp.int32)
        hidden_states = jax.random.normal(ks[1], (B, S, H), dtype=jnp.float32)
        W_down = jax.random.normal(ks[2], (E, H, BN), dtype=jnp.float32) * 0.02
        b_down = jnp.zeros((E, BN), dtype=jnp.float32)
        W_up = jax.random.normal(ks[3], (E, BN, H), dtype=jnp.float32) * 0.02
        b_up = jnp.zeros((E, H), dtype=jnp.float32)
        ln_w = jnp.ones((E, H), dtype=jnp.float32)
        ln_b = jnp.zeros((E, H), dtype=jnp.float32)
        return {'stream': stream, 'hidden_states': hidden_states, 'W_down': W_down, 'b_down': b_down, 'W_up': W_up, 'b_up': b_up, 'ln_w': ln_w, 'ln_b': ln_b}
    _L1_cond_all = _L1_cond_setup()
    _L1_cond_in = {k: v for k, v in _L1_cond_all.items() if k in ('W_down', 'b_down', 'W_up', 'b_up', 'ln_w', 'ln_b')}
    del _L1_cond_all
    return {'x': x, 'itok_B_1_2': itok_B_1_2, 'L0_cond_W_down': _L0_cond_in['W_down'], 'L0_cond_b_down': _L0_cond_in['b_down'], 'L0_cond_W_up': _L0_cond_in['W_up'], 'L0_cond_b_up': _L0_cond_in['b_up'], 'L0_cond_gamma': _L0_cond_in['gamma'], 'L0_cond_beta': _L0_cond_in['beta'], 'L1_cond_W_down': _L1_cond_in['W_down'], 'L1_cond_b_down': _L1_cond_in['b_down'], 'L1_cond_W_up': _L1_cond_in['W_up'], 'L1_cond_b_up': _L1_cond_in['b_up'], 'L1_cond_ln_w': _L1_cond_in['ln_w'], 'L1_cond_ln_b': _L1_cond_in['ln_b']}

def reference(x, itok_B_1_2, L0_cond_W_down, L0_cond_b_down, L0_cond_W_up, L0_cond_b_up, L0_cond_gamma, L0_cond_beta, L1_cond_W_down, L1_cond_b_down, L1_cond_W_up, L1_cond_b_up, L1_cond_ln_w, L1_cond_ln_b):
    import jax
    import jax.numpy as jnp

    def _L0_cond_ref(role, hidden_states, W_down, b_down, W_up, b_up, gamma, beta):
        import jax, jax.numpy as jnp
        import numpy as np
        H = 1024
        K = 512
        R = 3
        B = 8
        S = 1024
        LN_EPS = 1e-05
        h = jnp.einsum('bsh,bhk->bsk', hidden_states, W_down[role]) + b_down[role][:, None, :]
        h = jax.nn.gelu(h, approximate=False)
        u = jnp.einsum('bsk,bkh->bsh', h, W_up[role]) + b_up[role][:, None, :]
        y = hidden_states + u
        mean = jnp.mean(y, axis=-1, keepdims=True)
        var = jnp.mean(jnp.square(y - mean), axis=-1, keepdims=True)
        yn = (y - mean) * jax.lax.rsqrt(var + LN_EPS)
        return yn * gamma[role][:, None, :] + beta[role][:, None, :]

    def _L1_cond_ref(stream, hidden_states, W_down, b_down, W_up, b_up, ln_w, ln_b):
        import jax, jax.numpy as jnp
        import numpy as np
        B, S, H = (8, 1024, 1024)
        BN = 512
        E = 3
        LN_EPS = 1e-05
        Wd = W_down[stream]
        bd = b_down[stream]
        Wu = W_up[stream]
        bu = b_up[stream]
        g = ln_w[stream]
        b = ln_b[stream]
        residual = hidden_states
        h = jnp.einsum('bsh,bhk->bsk', hidden_states, Wd) + bd[:, None, :]
        h = jax.nn.gelu(h, approximate=False)
        h = jnp.einsum('bsk,bkh->bsh', h, Wu) + bu[:, None, :]
        h = residual + h
        mean = jnp.mean(h, axis=-1, keepdims=True)
        var = jnp.mean(jnp.square(h - mean), axis=-1, keepdims=True)
        h = (h - mean) * jax.lax.rsqrt(var + LN_EPS)
        return h * g[:, None, :] + b[:, None, :]
    x = _L0_cond_ref(itok_B_1_2, x, L0_cond_W_down, L0_cond_b_down, L0_cond_W_up, L0_cond_b_up, L0_cond_gamma, L0_cond_beta)
    x = _L1_cond_ref(itok_B_1_2, x, L1_cond_W_down, L1_cond_b_down, L1_cond_W_up, L1_cond_b_up, L1_cond_ln_w, L1_cond_ln_b)
    return x

_drawn_inputs = setup_inputs


def setup_inputs(seed=0):
    import zlib

    import numpy as np

    out = dict(_drawn_inputs(seed))
    spreads = {'L0_cond_gamma': (1.0, 0.2),
     'L0_cond_beta': (0.0, 0.1),
     'L1_cond_b_down': (0.0, 0.308),
     'L1_cond_b_up': (0.0, 0.1),
     'L1_cond_ln_w': (1.0, 0.2),
     'L1_cond_ln_b': (0.0, 0.1)}
    factors = {'L0_cond_b_down': 8.0}
    for name, (base, spread) in spreads.items():
        noise = np.random.default_rng([zlib.crc32(name.encode()), seed]).standard_normal(out[name].shape)
        drawn = base * np.exp(spread * noise) if base else spread * noise
        out[name] = jnp.asarray(drawn.astype(out[name].dtype))
    for name, factor in factors.items():
        out[name] = (out[name] * factor).astype(out[name].dtype)
    return out
```

```python
import concourse.bass as bass
import numpy as np
from concourse import mybir
from contextlib import ExitStack

NB = 128
H = 1024
K = 512
NU = 2 * NB
XB = 4
OB = 2
EPS = 1e-5


class Unit:

    def __init__(self, c, j=None, m=4):
        self.c, self.j, self.m = c, j, m

    def __add__(self, d):
        return Unit(self.c + d, self.j, self.m)

    def exists(self):
        return self.j is not None or 0 <= self.c < NU

    def value(self):
        return self.c if self.j is None else self.j * self.m + self.c

    def slot(self, n):
        return self.c % n

    def lap(self, n):
        k = self.c // n + 1
        return 16 * k if self.j is None else self.j * (16 * self.m // n) + 16 * k


def routed_adapters(nc, x, itok, Wd, bd, Wu, bu, ga, be, out):
    fp32 = mybir.dt.float32
    fp32r = mybir.dt.float32r
    i32 = mybir.dt.int32
    ALU = mybir.AluOpType
    ACT = mybir.ActivationFunctionType

    ctx = ExitStack()
    with ctx:
        def sb(name, shape, dt=fp32):
            return ctx.enter_context(nc.sbuf_tensor(name, shape, dt))

        def pb(name, shape):
            return ctx.enter_context(nc.psum_tensor(name, shape, fp32))

        def sem(name):
            return ctx.enter_context(nc.semaphore(name))

        wdh = sb("wdh", [128, 8, K], fp32r)
        wdl = sb("wdl", [128, 8, K], fp32r)
        wuh = sb("wuh", [128, 4, H], fp32r)
        wul = sb("wul", [128, 4, H], fp32r)
        rwd = sb("rwd", [128, 8, K])
        rwu = sb("rwu", [128, 4, H])
        rbd = sb("rbd", [128, K])
        rbu = sb("rbu", [128, H])
        rgb = sb("rgb", [128, 2, H])
        cbd = sb("cbd", [128, K])
        cbu = sb("cbu", [128, H])
        cgb = sb("cgb", [128, 2, H])

        xt = sb("xt", [128, XB, H])
        xr = sb("xr", [128, 2, H])
        xh = sb("xh", [128, H], fp32r)
        xl = sb("xl", [128, H], fp32r)
        hb = sb("hb", [128, K])
        hg = sb("hg", [128, K])
        hh = sb("hh", [128, K], fp32r)
        hl = sb("hl", [128, K], fp32r)
        y = sb("y", [128, 2, H])
        sq = sb("sq", [128, H])
        ot = sb("ot", [128, OB, H])
        ysum = sb("ysum", [128, 2])
        nmean = sb("nmean", [128, 2])
        ssq = sb("ssq", [128, 2])
        var = sb("var", [128, 2])
        rstd = sb("rstd", [128, 2])
        mhalf = sb("mhalf", [128, 1])
        heps = sb("heps", [128, 1])
        ones = sb("ones", [128, 1])
        ident = sb("ident", [128, 128])

        it_r = sb("it_r", [128, NB], i32)
        it_c = sb("it_c", [128, 1], i32)
        io_r = sb("io_r", [128, NB], i32)
        io_c = sb("io_c", [128, 1], i32)
        rf = sb("rf", [128, NB + 1])
        jf = sb("jf", [128, NB + 1])
        tf = sb("tf", [128, NB + 1])
        kf = sb("kf", [128, NB + 1])
        less = sb("less", [128, NB])
        pos = sb("pos", [128, 1])
        oneh = sb("oneh", [128, NB])
        qf = sb("qf", [1, NU])
        ff = sb("ff", [1, NU])
        c_ord = sb("c_ord", [1, NU], i32)
        c_q = sb("c_q", [1, NU], i32)
        c_new = sb("c_new", [1, NU], i32)

        pD = pb("pD", [128, K])
        pT = pb("pT", [128, H])
        pU = pb("pU", [128, H])
        pH = pb("pH", [128, K])
        pC = pb("pC", [128, 512])

        s_it = sem("s_it")
        s_io = sem("s_io")
        s_id = sem("s_id")
        s_p = sem("s_p")
        s_oh = sem("s_oh")
        s_pc = sem("s_pc")
        s_ctl = sem("s_ctl")
        s_rd = [sem(f"s_rd{g}") for g in range(4)]
        s_ru = [sem(f"s_ru{g}") for g in range(4)]
        s_rp = sem("s_rp")
        f_wd = sem("f_wd")
        f_wu = sem("f_wu")
        f_bd = sem("f_bd")
        f_gb = sem("f_gb")
        f_bu = sem("f_bu")
        s_wdh = sem("s_wdh")
        s_wuh = sem("s_wuh")
        s_x = [sem(f"s_x{k}") for k in range(XB)]
        s_st = [sem(f"s_st{k}") for k in range(OB)]
        s_r = sem("s_r")
        s_cb = sem("s_cb")
        s_T = sem("s_T")
        s_D = sem("s_D")
        s_U = sem("s_U")
        s_H = sem("s_H")
        s_xh = sem("s_xh")
        s_xl = sem("s_xl")
        s_hb = sem("s_hb")
        s_hg = sem("s_hg")
        s_hh = sem("s_hh")
        s_hl = sem("s_hl")
        s_y = sem("s_y")
        s_nm = sem("s_nm")
        s_sq = sem("s_sq")
        s_var = sem("s_var")
        s_rs = sem("s_rs")
        s_n = sem("s_n")
        s_o = sem("s_o")
        s_cd = sem("s_cd")
        s_cg = sem("s_cg")

        def done(eng, s, u):
            if u.exists():
                eng.wait_ge(s, u.value() + 1)

        def steps(eng, body):
            for c in range(3):
                body(Unit(c))
            with eng.Fori(0, (NU - 4) // 4) as j:
                for m in range(4):
                    body(Unit(3 + m, j))
            for c in range(NU - 1, NU + 1):
                body(Unit(c))

        def new_phase(eng, u):
            return eng.value_load(c_new[0:1, bass.ds(u.value(), 1)], min_val=0, max_val=1)

        class Phases:

            def __init__(self, eng, name):
                self.eng = eng
                self.reg = eng.alloc_register(name)
                eng.reg_mov(self.reg, 0)

            def next(self):
                before = self.eng.snap(self.reg)
                self.eng.reg_add(self.reg, self.reg, 1)
                return before

        block = ctx.enter_context(nc.Block())

        @block.sync
        def _(eng):
            eng.dma_start(it_r[:, :], itok.rearrange("(a n) -> a n", a=1).broadcast_to([128, NB])).then_inc(s_it, 16)
            eng.dma_start(it_c[:, :], itok.rearrange("(n a) -> n a", a=1)).then_inc(s_it, 16)
            eng.wait_ge(s_ctl, 1)
            phases = Phases(eng, "sp_ph")

            def load_phase(u):
                q = eng.value_load(c_q[0:1, bass.ds(u.value(), 1)], min_val=0, max_val=5)
                c = phases.next()
                row = bass.ds(q, 1)
                eng.wait_ge(f_wd, c + 1)
                for g in range(4):
                    eng.dma_start(rwd[:, 2 * g:2 * g + 2, :],
                                  Wd[row, 256 * g:256 * g + 256, :].rearrange("a (k p) n -> (a p) k n", p=128))\
                       .then_inc(s_rd[g], 16)
                eng.wait_ge(f_bd, c + 1)
                eng.wait_ge(f_bu, c + 1)
                eng.wait_ge(f_gb, c + 1)
                eng.dma_start(rbd[:, :], bd[row, :].broadcast_to([128, K])).then_inc(s_rp, 16)
                eng.dma_start(rbu[:, :], bu[row, :].broadcast_to([128, H])).then_inc(s_rp, 16)
                eng.wait_ge(f_wu, c + 1)
                for g in range(4):
                    eng.dma_start(rwu[:, g:g + 1, :],
                                  Wu[row, 128 * g:128 * g + 128, :].rearrange("a (k p) n -> (a p) k n", p=128))\
                       .then_inc(s_ru[g], 16)
                eng.dma_start(rgb[:, 0, :], ga[row, :].broadcast_to([128, H])).then_inc(s_rp, 16)
                eng.dma_start(rgb[:, 1, :], be[row, :].broadcast_to([128, H])).then_inc(s_rp, 16)

            def load(u, src):
                if u.j is None and u.c == 0:
                    load_x(u, src)
                    load_phase(u)
                else:
                    with eng.If(new_phase(eng, u) == 1):
                        load_phase(u)
                    load_x(u, src)

            def load_x(u, src):
                o = eng.value_load(c_ord[0:1, bass.ds(u.value(), 1)], min_val=0, max_val=NB - 1)
                if u.j is not None or u.c >= XB:
                    done(eng, s_T, u + -XB)
                    done(eng, s_r, u + -XB)
                eng.dma_start(xt[:, u.slot(XB), :], src[bass.ds(o, 1), :, :].rearrange("a p n -> (a p) n"))\
                   .then_inc(s_x[u.slot(XB)], 16)

            for c in range(XB):
                load(Unit(c), x)
            with eng.Fori(0, (NB - XB) // 4) as j:
                for m in range(4):
                    load(Unit(XB + m, j), x)
            with eng.Fori(0, NB // 4) as j:
                for m in range(4):
                    eng.wait_ge(s_st[m % OB], Unit(m, j).lap(OB))
                    load(Unit(NB + m, j), out)

        @block.gpsimd
        def _(eng):
            eng.iota(io_r[:, :], pattern=[[1, NB]], base=0, channel_multiplier=0).then_inc(s_io, 1)
            eng.iota(io_c[:, :], pattern=[[1, 1]], base=0, channel_multiplier=1).then_inc(s_io, 1)
            eng.memset(mhalf[:, :], -0.5).then_inc(s_id, 1)
            eng.memset(heps[:, :], H * EPS)
            eng.memset(ones[:, :], 1.0)
            eng.memset(ident[:, :], 0.0).then_inc(s_id, 1)
            eng.wait_ge(s_id, 2)
            eng.affine_select(out=ident[:, :], in_=ident[:, :], compare_op=ALU.not_equal, fill=1.0, base=0,
                              pattern=[[-1, 128]], channel_multiplier=1).then_inc(s_id, 1)
            eng.sem_inc(f_bu, 1)
            eng.wait_ge(s_ctl, 1)
            phases = Phases(eng, "pl_ph")

            def take_bu(c):
                eng.wait_ge(s_rp, c * 64 + 64)
                eng.tensor_tensor(cbu[:, :], rbu[:, :], ones[:, 0:1].broadcast_to([128, H]), ALU.mult).then_inc(f_bu, 1)

            def residual(u):
                if u.j is None and u.c == 0:
                    take_bu(phases.next())
                else:
                    with eng.If(new_phase(eng, u) == 1):
                        take_bu(phases.next())
                eng.drain().then_inc(s_cb, 1)
                done(eng, s_cb, u)
                eng.wait_ge(s_x[u.slot(XB)], u.lap(XB))
                done(eng, s_y, u + -2)
                eng.tensor_tensor(xr[:, u.slot(2), :], xt[:, u.slot(XB), :], cbu[:, :], ALU.add).then_inc(s_r, 1)

            def body(i):
                if i.j is None and i.c == 0:
                    residual(i)
                if i.j is not None or i.c + 1 < NU:
                    residual(i + 1)
                v = i + -1
                if v.exists():
                    k = v.slot(2)
                    done(eng, s_sq, v)
                    eng.tensor_tensor(var[:, k:k + 1], ssq[:, k:k + 1], heps[:, :], ALU.add).then_inc(s_var, 1)
                    done(eng, s_var, v)
                    eng.tensor_tensor(rstd[:, k:k + 1], var[:, k:k + 1], mhalf[:, :], ALU.pow).then_inc(s_rs, 1)

            steps(eng, body)

        @block.tensor
        def _(eng):
            eng.wait_ge(s_oh, 1)
            eng.matmul(pC[0:1, 0:NB], jf[:, NB:NB + 1], oneh[:, :], start=True, stop=True)
            eng.matmul(pC[0:1, NB:NU], rf[:, NB:NB + 1], oneh[:, :], start=True, stop=True).then_inc(s_pc, 1)
            eng.wait_ge(s_id, 3)

            def transpose_x(u):
                eng.wait_ge(s_x[u.slot(XB)], u.lap(XB))
                for k in range(8):
                    last = eng.transpose(pT[:, 128 * k:128 * k + 128], xt[:, u.slot(XB), 128 * k:128 * k + 128],
                                         ident[:, :])
                last.then_inc(s_T, 1)

            def body(i):
                if i.j is None and i.c == 0:
                    transpose_x(i)
                if i.exists():
                    done(eng, s_xh, i)
                    done(eng, s_xl, i)
                    n = 0
                    for k in range(8):
                        for a, w in ((xh, wdh), (xh, wdl), (xl, wdh)):
                            last = eng.matmul(pD[:, :], a[:, 128 * k:128 * k + 128], w[:, k, :],
                                              start=(n == 0), stop=(n == 23))
                            n += 1
                    last.then_inc(s_D, 1)
                if i.j is not None or i.c + 1 < NU:
                    transpose_x(i + 1)
                v = i + -1
                if v.exists():
                    done(eng, s_hh, v)
                    done(eng, s_hl, v)
                    for m in range(2):
                        n = 0
                        for k in range(4):
                            for a, w in ((hh, wuh), (hh, wul), (hl, wuh)):
                                last = eng.matmul(pU[:, K * m:K * m + K], a[:, 128 * k:128 * k + 128],
                                                  w[:, k, K * m:K * m + K], start=(n == 0), stop=(n == 11))
                                n += 1
                    last.then_inc(s_U, 1)
                if i.exists():
                    done(eng, s_hg, i)
                    for k in range(4):
                        last = eng.transpose(pH[:, 128 * k:128 * k + 128], hg[:, 128 * k:128 * k + 128], ident[:, :])
                    last.then_inc(s_H, 1)

            steps(eng, body)

        @block.scalar
        def _(eng):
            eng.wait_ge(s_ctl, 1)
            pd = Phases(eng, "ac_pd")
            pu = Phases(eng, "ac_pu")

            def take_wd(i):
                c = pd.next()
                done(eng, s_D, i + -1)
                for g in range(4):
                    eng.wait_ge(s_rd[g], c * 16 + 16)
                    eng.activation(wdh[:, 2 * g:2 * g + 2, :], rwd[:, 2 * g:2 * g + 2, :], ACT.Copy)\
                       .then_inc(s_wdh, 1)

            def take_wu(i):
                c = pu.next()
                done(eng, s_U, i + -1)
                for g in range(4):
                    eng.wait_ge(s_ru[g], c * 16 + 16)
                    eng.activation(wuh[:, g:g + 1, :], rwu[:, g:g + 1, :], ACT.Copy).then_inc(s_wuh, 1)

            def split_x(u):
                if u.j is None and u.c == 0:
                    take_wd(u)
                else:
                    with eng.If(new_phase(eng, u) == 1):
                        take_wd(u)
                done(eng, s_T, u)
                done(eng, s_D, u + -1)
                eng.activation(xh[:, :], pT[:, :], ACT.Copy).then_inc(s_xh, 1)

            def body(i):
                if i.j is None and i.c == 0:
                    split_x(i)
                if i.exists():
                    done(eng, s_hb, i)
                    done(eng, s_H, i + -1)
                    eng.activation(hg[:, :], hb[:, :], ACT.Gelu).then_inc(s_hg, 1)
                if i.j is not None or i.c + 1 < NU:
                    split_x(i + 1)
                if i.exists():
                    if i.j is None and i.c == 0:
                        take_wu(i)
                    else:
                        with eng.If(new_phase(eng, i) == 1):
                            take_wu(i)
                    done(eng, s_H, i)
                    done(eng, s_U, i + -1)
                    eng.activation(hh[:, :], pH[:, :], ACT.Copy).then_inc(s_hh, 1)
                v = i + -1
                if v.exists():
                    k = v.slot(2)
                    done(eng, s_nm, v)
                    done(eng, s_rs, v + -2)
                    eng.activation(sq[:, :], y[:, k, :], ACT.Square, bias=nmean[:, k:k + 1],
                                   accum_out=ssq[:, k:k + 1]).then_inc(s_sq, 1)
                w = i + -2
                if w.exists():
                    store(w)
                if i.j is None and i.c == NU:
                    store(i + -1)

            def store(w):
                o = eng.value_load(c_ord[0:1, bass.ds(w.value(), 1)], min_val=0, max_val=NB - 1)
                done(eng, s_o, w)
                eng.dma_start(out[bass.ds(o, 1), :, :].rearrange("a p n -> (a p) n"), ot[:, w.slot(OB), :])\
                   .then_inc(s_st[w.slot(OB)], 16)

            steps(eng, body)
            for k in range(OB):
                eng.wait_ge(s_st[k], 16 * NU // OB)

        @block.vector
        def _(eng):
            chain = [0]

            def link(ins):
                chain[0] += 1
                ins.then_inc(s_p, 1)
                eng.wait_ge(s_p, chain[0])

            eng.wait_ge(s_it, 32)
            eng.wait_ge(s_io, 2)
            link(eng.tensor_copy(rf[:, 0:NB], it_r[:, :]))
            link(eng.tensor_copy(rf[:, NB:NB + 1], it_c[:, :]))
            link(eng.tensor_copy(jf[:, 0:NB], io_r[:, :]))
            link(eng.tensor_copy(jf[:, NB:NB + 1], io_c[:, :]))
            link(eng.tensor_scalar(tf[:, :], rf[:, :], 0.0, 3.0, ALU.is_lt, ALU.mult))
            link(eng.tensor_tensor(tf[:, :], tf[:, :], rf[:, :], ALU.add))
            link(eng.tensor_scalar(rf[:, :], tf[:, :], 0.0, 2.0, ALU.max, ALU.min))
            link(eng.scalar_tensor_tensor(out=kf[:, :], in0=rf[:, :], scalar=float(NB), in1=jf[:, :],
                                          op0=ALU.mult, op1=ALU.add))
            link(eng.tensor_scalar(less[:, :], kf[:, 0:NB], kf[:, NB:NB + 1], None, ALU.is_lt))
            link(eng.reduce_sum(pos[:, :], less[:, :], mybir.AxisListType.X))
            eng.tensor_scalar(oneh[:, :], jf[:, 0:NB], pos[:, 0:1], None, ALU.is_equal).then_inc(s_oh, 1)
            eng.wait_ge(s_pc, 1)
            link(eng.tensor_copy(c_ord[:, 0:NB], pC[0:1, 0:NB]))
            link(eng.tensor_copy(c_ord[:, NB:NU], pC[0:1, 0:NB]))
            link(eng.tensor_copy(qf[:, 0:NB], pC[0:1, NB:NU]))
            link(eng.tensor_scalar(qf[:, NB:NU], pC[0:1, NB:NU], 3.0, None, ALU.add))
            link(eng.tensor_copy(c_q[:, :], qf[:, :]))
            link(eng.memset(ff[:, 0:1], 1.0))
            link(eng.tensor_tensor(ff[:, 1:NU], qf[:, 1:NU], qf[:, 0:NU - 1], ALU.not_equal))
            eng.tensor_copy(c_new[:, :], ff[:, :]).then_inc(s_ctl, 1)
            for s in (f_wd, f_wu, f_bd, f_gb):
                eng.sem_inc(s, 1)
            eng.wait_ge(s_ctl, 1)
            pd = Phases(eng, "ve_pd")
            pu = Phases(eng, "ve_pu")
            pg = Phases(eng, "ve_pg")

            def take_wd(i):
                c = pd.next()
                done(eng, s_D, i + -1)
                done(eng, s_hb, i + -1)
                eng.wait_ge(s_rp, c * 64 + 64)
                eng.tensor_copy(cbd[:, :], rbd[:, :]).then_inc(f_bd, 1)
                for g in range(4):
                    eng.wait_ge(s_wdh, c * 4 + (g + 1))
                    s = slice(2 * g, 2 * g + 2)
                    last = eng.tensor_tensor(wdl[:, s, :], rwd[:, s, :], wdh[:, s, :].bitcast(fp32), ALU.subtract)
                last.then_inc(f_wd, 1)

            def take_wu(i):
                c = pu.next()
                done(eng, s_U, i + -1)
                for g in range(4):
                    eng.wait_ge(s_wuh, c * 4 + (g + 1))
                    s = slice(g, g + 1)
                    last = eng.tensor_tensor(wul[:, s, :], rwu[:, s, :], wuh[:, s, :].bitcast(fp32), ALU.subtract)
                last.then_inc(f_wu, 1)

            def take_gb():
                c = pg.next()
                eng.wait_ge(s_rp, c * 64 + 64)
                eng.tensor_scalar(cgb[:, 0, :], rgb[:, 0, :], float(H) ** 0.5, None, ALU.mult)
                eng.tensor_copy(cgb[:, 1, :], rgb[:, 1, :]).then_inc(f_gb, 1)

            def split_x(u):
                if u.j is None and u.c == 0:
                    take_wd(u)
                else:
                    with eng.If(new_phase(eng, u) == 1):
                        take_wd(u)
                done(eng, s_xh, u)
                eng.tensor_tensor(xl[:, :], pT[:, :], xh[:, :].bitcast(fp32), ALU.subtract).then_inc(s_xl, 1)

            def body(i):
                if i.j is None and i.c == 0:
                    split_x(i)
                if i.exists():
                    done(eng, s_D, i)
                    done(eng, s_xl, i)
                    done(eng, s_hg, i + -1)
                    eng.tensor_tensor(hb[:, :], pD[:, :], cbd[:, :], ALU.add).then_inc(s_hb, 1)
                if i.j is not None or i.c + 1 < NU:
                    split_x(i + 1)
                v = i + -1
                k = v.slot(2)
                if v.exists():
                    done(eng, s_U, v)
                    done(eng, s_r, v)
                    eng.scalar_tensor_tensor(out=y[:, k, :], in0=pU[:, :], scalar=1.0, in1=xr[:, k, :],
                                             op0=ALU.mult, op1=ALU.add, accum_out=ysum[:, k:k + 1]).then_inc(s_y, 1)
                    done(eng, s_y, v)
                    eng.tensor_scalar(nmean[:, k:k + 1], ysum[:, k:k + 1], -1.0 / H, None, ALU.mult)\
                       .then_inc(s_nm, 1)
                if i.exists():
                    if i.j is None and i.c == 0:
                        new = None
                        take_wu(i)
                    else:
                        new = new_phase(eng, i)
                        with eng.If(new == 1):
                            take_wu(i)
                    done(eng, s_hh, i)
                    eng.tensor_tensor(hl[:, :], pH[:, :], hh[:, :].bitcast(fp32), ALU.subtract).then_inc(s_hl, 1)
                if v.exists():
                    o = v.slot(OB)
                    if v.j is not None or v.c >= OB:
                        eng.wait_ge(s_st[o], (v + -OB).lap(OB))
                    done(eng, s_nm, v)
                    eng.scalar_tensor_tensor(out=ot[:, o, :], in0=y[:, k, :], scalar=nmean[:, k:k + 1],
                                             in1=cgb[:, 0, :], op0=ALU.add, op1=ALU.mult).then_inc(s_n, 1)
                    done(eng, s_rs, v)
                    done(eng, s_n, v)
                    eng.scalar_tensor_tensor(out=ot[:, o, :], in0=ot[:, o, :], scalar=rstd[:, k:k + 1],
                                             in1=cgb[:, 1, :], op0=ALU.mult, op1=ALU.add).then_inc(s_o, 1)
                if i.exists():
                    if i.j is None and i.c == 0:
                        take_gb()
                    else:
                        with eng.If(new == 1):
                            done(eng, s_o, i + -1)
                            take_gb()

            steps(eng, body)


_OUT = ((NB, 128, H), "float32")


def kernel(x, itok_B_1_2, L0_cond_W_down, L0_cond_b_down, L0_cond_W_up, L0_cond_b_up, L0_cond_gamma, L0_cond_beta,
           L1_cond_W_down, L1_cond_b_down, L1_cond_W_up, L1_cond_b_up, L1_cond_ln_w, L1_cond_ln_b):
    import concourse.bacc as bacc
    from concourse.bass_utils import run_bass_kernel_spmd

    given = {
        "x": x,
        "itok": itok_B_1_2,
        "Wd": np.concatenate([L0_cond_W_down, L1_cond_W_down]),
        "bd": np.concatenate([L0_cond_b_down, L1_cond_b_down]),
        "Wu": np.concatenate([L0_cond_W_up, L1_cond_W_up]),
        "bu": np.concatenate([L0_cond_b_up, L1_cond_b_up]),
        "ga": np.concatenate([L0_cond_gamma, L1_cond_ln_w]),
        "be": np.concatenate([L0_cond_beta, L1_cond_ln_b]),
    }
    nc = bacc.Bacc("TRN2", target_bir_lowering=False, num_devices=1)
    arrays, args = {}, []
    for name, a in given.items():
        a = np.ascontiguousarray(a)
        arrays[f"in_{name}"] = a
        args.append(nc.dram_tensor(f"in_{name}", a.shape, mybir.dt.from_np(a.dtype), kind="ExternalInput").ap())
    out = nc.dram_tensor("out_0", _OUT[0], mybir.dt.from_np(np.dtype(_OUT[1])), kind="ExternalOutput").ap()
    routed_adapters(nc, *args, out)
    r = run_bass_kernel_spmd(nc, [arrays], core_ids=[0])
    return r.results[0]["out_0"]
```

```python
import concourse.bass as bass
import numpy as np
from concourse import mybir
from contextlib import ExitStack

NB = 128
H = 1024
K = 512
NU = 2 * NB
XB = 4
QB = 2
OB = 2
EPS = 1e-5


class Unit:

    def __init__(self, c, j=None, m=4):
        self.c, self.j, self.m = c, j, m

    def __add__(self, d):
        return Unit(self.c + d, self.j, self.m)

    def exists(self):
        return self.j is not None or 0 <= self.c < NU

    def value(self):
        return self.c if self.j is None else self.j * self.m + self.c

    def slot(self, n):
        return self.c % n

    def lap(self, n):
        k = self.c // n + 1
        return 16 * k if self.j is None else self.j * (16 * self.m // n) + 16 * k


def routed_adapters(nc, x, itok, Wd, bd, Wu, bu, ga, be, out):
    fp32 = mybir.dt.float32
    fp32r = mybir.dt.float32r
    i32 = mybir.dt.int32
    ALU = mybir.AluOpType
    ACT = mybir.ActivationFunctionType

    ctx = ExitStack()
    with ctx:
        def sb(name, shape, dt=fp32):
            return ctx.enter_context(nc.sbuf_tensor(name, shape, dt))

        def pb(name, shape):
            return ctx.enter_context(nc.psum_tensor(name, shape, fp32))

        def sem(name):
            return ctx.enter_context(nc.semaphore(name))

        wdh = sb("wdh", [128, 8, K], fp32r)
        wdl = sb("wdl", [128, 8, K], fp32r)
        wuh = sb("wuh", [128, 4, H], fp32r)
        wul = sb("wul", [128, 4, H], fp32r)
        rwd = sb("rwd", [128, 8, K])
        rwu = sb("rwu", [128, 4, H])
        rbd = sb("rbd", [128, K])
        rbu = sb("rbu", [128, H])
        rgb = sb("rgb", [128, 2, H])
        cbd = sb("cbd", [128, K])
        cbu = sb("cbu", [128, H])
        cgb = sb("cgb", [128, 2, H])

        xt = sb("xt", [128, XB, H])
        xq = sb("xq", [128, QB, 4, 256])
        xT = sb("xT", [128, 8, 4, 32])
        xh = sb("xh", [128, 2, H], fp32r)
        xl = sb("xl", [128, 2, H], fp32r)
        hb = sb("hb", [128, K])
        hg = sb("hg", [128, 2, K])
        hq = sb("hq", [128, 2, 4, 128])
        hT = sb("hT", [128, 4, 4, 32])
        hh = sb("hh", [128, K], fp32r)
        hl = sb("hl", [128, K], fp32r)
        y = sb("y", [128, H])
        ot = sb("ot", [128, OB, H])
        ysum = sb("ysum", [128, 2])
        nmean = sb("nmean", [128, 2])
        ssq = sb("ssq", [128, 2])
        var = sb("var", [128, 2])
        rstd = sb("rstd", [128, 2])
        mhalf = sb("mhalf", [128, 1])
        htok = nc.dram_tensor("htok", [2, 128, K], fp32).ap()
        heps = sb("heps", [128, 1])
        ones = sb("ones", [128, 1])

        it_r = sb("it_r", [128, NB], i32)
        it_c = sb("it_c", [128, 1], i32)
        io_r = sb("io_r", [128, NB], i32)
        io_c = sb("io_c", [128, 1], i32)
        rf, jf, tf, kf = (ot[:, 0, (NB + 1) * n:(NB + 1) * (n + 1)] for n in range(4))
        less, oneh = (ot[:, 1, NB * n:NB * (n + 1)] for n in range(2))
        qf, ff = (ot[0:1, 1, NU * n:NU * (n + 1)] for n in range(1, 3))
        pos = sb("pos", [128, 1])
        c_ord = sb("c_ord", [1, NU], i32)
        c_q = sb("c_q", [1, NU], i32)
        c_new = sb("c_new", [1, NU], i32)

        pD = pb("pD", [128, K])
        pU = pb("pU", [128, H])
        sq = pb("sq", [128, H])
        pC = pb("pC", [128, 512])

        s_it = sem("s_it")
        s_io = sem("s_io")
        s_id = sem("s_id")
        s_p = sem("s_p")
        s_oh = sem("s_oh")
        s_pc = sem("s_pc")
        s_ctl = sem("s_ctl")
        s_rd = [sem(f"s_rd{g}") for g in range(4)]
        s_ru = [sem(f"s_ru{g}") for g in range(4)]
        s_rbd = sem("s_rbd")
        s_rbu = sem("s_rbu")
        s_rgb = sem("s_rgb")
        f_wd = sem("f_wd")
        f_wu = sem("f_wu")
        f_bd = sem("f_bd")
        f_gb = sem("f_gb")
        f_bu = sem("f_bu")
        s_wdh = sem("s_wdh")
        s_wuh = sem("s_wuh")
        s_x = [sem(f"s_x{k}") for k in range(XB)]
        s_st = [sem(f"s_st{k}") for k in range(OB)]
        s_r = sem("s_r")
        s_cb = sem("s_cb")
        s_xq = [sem(f"s_xq{k}") for k in range(QB)]
        s_T = sem("s_T")
        s_D = sem("s_D")
        s_U = sem("s_U")
        s_hs = [sem(f"s_hs{k}") for k in range(2)]
        s_hq = [sem(f"s_hq{k}") for k in range(2)]
        s_H = sem("s_H")
        s_xh = sem("s_xh")
        s_xl = sem("s_xl")
        s_hb = sem("s_hb")
        s_hg = sem("s_hg")
        s_hh = sem("s_hh")
        s_hl = sem("s_hl")
        s_y = sem("s_y")
        s_nm = sem("s_nm")
        s_sq = sem("s_sq")
        s_var = sem("s_var")
        s_rs = sem("s_rs")
        s_n = sem("s_n")
        s_o = sem("s_o")
        s_cd = sem("s_cd")
        s_cg = sem("s_cg")

        def done(eng, s, u):
            if u.exists():
                eng.wait_ge(s, u.value() + 1)

        def steps(eng, body):
            for c in range(4):
                body(Unit(c))
            with eng.Fori(0, NU // 4 - 2) as j:
                for m in range(4):
                    body(Unit(4 + m, j))
            for c in range(NU - 4, NU + 2):
                body(Unit(c))

        def new_phase(eng, u):
            return eng.value_load(c_new[0:1, bass.ds(u.value(), 1)], min_val=0, max_val=1)

        class Phases:

            def __init__(self, eng, name):
                self.eng = eng
                self.reg = eng.alloc_register(name)
                eng.reg_mov(self.reg, 0)

            def next(self):
                before = self.eng.snap(self.reg)
                self.eng.reg_add(self.reg, self.reg, 1)
                return before

        block = ctx.enter_context(nc.Block())

        @block.sync
        def _(eng):
            eng.dma_start(it_r[:, :], itok.rearrange("(a n) -> a n", a=1).broadcast_to([128, NB])).then_inc(s_it, 16)
            eng.dma_start(it_c[:, :], itok.rearrange("(n a) -> n a", a=1)).then_inc(s_it, 16)
            eng.wait_ge(s_ctl, 1)
            pd = Phases(eng, "sp_pd")
            pu = Phases(eng, "sp_pu")

            def load_down(u):
                q = eng.value_load(c_q[0:1, bass.ds(u.value(), 1)], min_val=0, max_val=5)
                c = pd.next()
                row = bass.ds(q, 1)
                eng.wait_ge(f_wd, c + 1)
                for g in range(4):
                    for a in range(4):
                        eng.dma_start(rwd[32 * a:32 * a + 32, 2 * g:2 * g + 2, :],
                                      Wd[row, 256 * a + 64 * g:256 * a + 64 * g + 64, :]
                                      .rearrange("a (k i) n -> (a i) k n", i=32)).then_inc(s_rd[g], 16)
                eng.wait_ge(f_bd, c + 1)
                eng.dma_start(rbd[:, :], bd[row, :].broadcast_to([128, K])).then_inc(s_rbd, 16)
                eng.wait_ge(f_bu, c + 1)
                eng.dma_start(rbu[:, :], bu[row, :].broadcast_to([128, H])).then_inc(s_rbu, 16)

            def load_up(u):
                q = eng.value_load(c_q[0:1, bass.ds(u.value(), 1)], min_val=0, max_val=5)
                c = pu.next()
                row = bass.ds(q, 1)
                eng.wait_ge(f_wu, c + 1)
                for g in range(4):
                    for a in range(4):
                        eng.dma_start(rwu[32 * a:32 * a + 32, g, :],
                                      Wu[row, 128 * a + 32 * g:128 * a + 32 * g + 32, :]
                                      .rearrange("a i n -> (a i) n")).then_inc(s_ru[g], 16)
                eng.wait_ge(f_gb, c + 1)
                eng.dma_start(rgb[:, 0, :], ga[row, :].broadcast_to([128, H])).then_inc(s_rgb, 16)
                eng.dma_start(rgb[:, 1, :], be[row, :].broadcast_to([128, H])).then_inc(s_rgb, 16)

            def load_q(u, src):
                o = eng.value_load(c_ord[0:1, bass.ds(u.value(), 1)], min_val=0, max_val=NB - 1)
                k = u.slot(QB)
                done(eng, s_T, u + -QB)
                for a in range(4):
                    eng.dma_start(xq[32 * a:32 * a + 32, k, :, :],
                                  src[bass.ds(o, 1), :, 256 * a:256 * a + 256]
                                  .rearrange("a (b j) n -> (a j) b n", j=32)).then_inc(s_xq[k], 16)

            def load_t(u, src):
                o = eng.value_load(c_ord[0:1, bass.ds(u.value(), 1)], min_val=0, max_val=NB - 1)
                k = u.slot(XB)
                done(eng, s_y, u + -XB)
                eng.dma_start(xt[:, k, :], src[bass.ds(o, 1), :, :].rearrange("a p n -> (a p) n"))\
                   .then_inc(s_x[k], 16)

            def maybe_up(u):
                if u.j is None and u.c == 0:
                    load_up(u)
                elif u.exists():
                    with eng.If(new_phase(eng, u) == 1):
                        load_up(u)

            def load(u, src, before):
                t = u + -1
                load_q(u, src)
                if t.exists():
                    load_t(t, before)
                if u.j is None and u.c == 0:
                    load_down(u)
                else:
                    with eng.If(new_phase(eng, u) == 1):
                        load_down(u)
                maybe_up(u + -2)

            for c in range(XB + 1):
                load(Unit(c), x, x)
            with eng.Fori(0, (NB - 8) // 4) as j:
                for m in range(4):
                    load(Unit(XB + 1 + m, j), x, x)
            for c in range(NB - 3, NB):
                load(Unit(c), x, x)
            for c in range(NB, NB + 4):
                eng.wait_ge(s_st[c % OB], Unit(c - NB).lap(OB))
                load(Unit(c), out, x if c == NB else out)
            with eng.Fori(0, NB // 4 - 1) as j:
                for m in range(4):
                    eng.wait_ge(s_st[m % OB], Unit(4 + m, j).lap(OB))
                    load(Unit(NB + 4 + m, j), out, out)
            load_t(Unit(NU - 1), out)
            maybe_up(Unit(NU - 2))
            maybe_up(Unit(NU - 1))

        @block.gpsimd
        def _(eng):
            eng.iota(io_r[:, :], pattern=[[1, NB]], base=0, channel_multiplier=0).then_inc(s_io, 1)
            eng.iota(io_c[:, :], pattern=[[1, 1]], base=0, channel_multiplier=1).then_inc(s_io, 1)
            eng.memset(mhalf[:, :], -0.5).then_inc(s_id, 1)
            eng.memset(heps[:, :], H * EPS).then_inc(s_id, 1)
            eng.memset(ones[:, :], 1.0).then_inc(s_id, 1)
            eng.wait_ge(s_id, 3)
            eng.sem_inc(f_bu, 1)
            eng.wait_ge(s_ctl, 1)
            phases = Phases(eng, "pl_ph")

            def take_bu(u, c):
                done(eng, s_r, u + -1)
                eng.wait_ge(s_rbu, c * 16 + 16)
                eng.tensor_tensor(cbu[:, :], rbu[:, :], ones[:, 0:1].broadcast_to([128, H]), ALU.mult).then_inc(f_bu, 1)

            def residual(u):
                if u.j is None and u.c == 0:
                    take_bu(u, phases.next())
                else:
                    with eng.If(new_phase(eng, u) == 1):
                        take_bu(u, phases.next())
                eng.drain().then_inc(s_cb, 1)
                done(eng, s_cb, u)
                eng.wait_ge(s_x[u.slot(XB)], u.lap(XB))
                eng.tensor_tensor(xt[:, u.slot(XB), :], xt[:, u.slot(XB), :], cbu[:, :], ALU.add).then_inc(s_r, 1)

            def body(i):
                if i.exists():
                    residual(i)
                v = i + -2
                if v.exists():
                    k = v.slot(2)
                    done(eng, s_sq, v)
                    eng.tensor_tensor(var[:, k:k + 1], ssq[:, k:k + 1], heps[:, :], ALU.add).then_inc(s_var, 1)
                    done(eng, s_var, v)
                    eng.tensor_tensor(rstd[:, k:k + 1], var[:, k:k + 1], mhalf[:, :], ALU.pow).then_inc(s_rs, 1)

            steps(eng, body)

        @block.tensor
        def _(eng):
            eng.wait_ge(s_oh, 1)
            eng.matmul(pC[0:1, 0:NB], jf[:, NB:NB + 1], oneh[:, :], start=True, stop=True)
            eng.matmul(pC[0:1, NB:NU], rf[:, NB:NB + 1], oneh[:, :], start=True, stop=True).then_inc(s_pc, 1)

            def body(i):
                if i.exists():
                    done(eng, s_xh, i)
                    done(eng, s_xl, i)
                    n = 0
                    b = i.slot(2)
                    for k in range(8):
                        for a, w in ((xh, wdh), (xh, wdl), (xl, wdh)):
                            last = eng.matmul(pD[:, :], a[:, b, 128 * k:128 * k + 128], w[:, k, :],
                                              start=(n == 0), stop=(n == 23))
                            n += 1
                    last.then_inc(s_D, 1)
                v = i + -2
                if v.exists():
                    done(eng, s_hh, v)
                    done(eng, s_hl, v)
                    for m in range(2):
                        n = 0
                        for k in range(4):
                            for a, w in ((hh, wuh), (hh, wul), (hl, wuh)):
                                last = eng.matmul(pU[:, K * m:K * m + K], a[:, 128 * k:128 * k + 128],
                                                  w[:, k, K * m:K * m + K], start=(n == 0), stop=(n == 11))
                                n += 1
                    last.then_inc(s_U, 1)

            steps(eng, body)

        @block.scalar
        def _(eng):
            eng.wait_ge(s_ctl, 1)
            pd = Phases(eng, "ac_pd")
            pu = Phases(eng, "ac_pu")

            def take_wd(i):
                c = pd.next()
                done(eng, s_D, i + -1)
                for g in range(4):
                    eng.wait_ge(s_rd[g], c * 64 + 64)
                    eng.activation(wdh[:, 2 * g:2 * g + 2, :], rwd[:, 2 * g:2 * g + 2, :], ACT.Copy)\
                       .then_inc(s_wdh, 1)

            def take_wu(i):
                c = pu.next()
                done(eng, s_U, i + -1)
                for g in range(4):
                    eng.wait_ge(s_ru[g], c * 64 + 64)
                    eng.activation(wuh[:, g:g + 1, :], rwu[:, g:g + 1, :], ACT.Copy).then_inc(s_wuh, 1)

            def split_x(u):
                if u.j is None and u.c == 0:
                    take_wd(u)
                else:
                    with eng.If(new_phase(eng, u) == 1):
                        take_wd(u)
                done(eng, s_T, u)
                done(eng, s_D, u + -2)
                eng.activation(xh[:, u.slot(2), :], xT[:, :, :, :].rearrange("p k b j -> p (k b j)"), ACT.Copy).then_inc(s_xh, 1)

            def take_wu_and_split_h(p):
                if p.j is None and p.c == 0:
                    take_wu(p)
                else:
                    with eng.If(new_phase(eng, p) == 1):
                        take_wu(p)
                done(eng, s_H, p)
                done(eng, s_U, p + -1)
                eng.activation(hh[:, :], hT[:, :, :, :].rearrange("p k b j -> p (k b j)"), ACT.Copy)\
                   .then_inc(s_hh, 1)

            def body(i):
                if i.j is None and i.c == 0:
                    split_x(i)
                if i.j is not None or i.c + 1 < NU:
                    split_x(i + 1)
                h = i.slot(2)
                if i.exists():
                    done(eng, s_hb, i)
                    if (i + -2).exists():
                        eng.wait_ge(s_hs[h], (i + -2).lap(2))
                    eng.activation(hg[:, h, :], hb[:, :], ACT.Gelu).then_inc(s_hg, 1)
                    if (i + -2).exists():
                        eng.wait_ge(s_hq[h], (i + -2).lap(2) * 4)
                    done(eng, s_hg, i)
                    eng.dma_start(htok[h, :, :], hg[:, h, :]).then_inc(s_hs[h], 16)
                p = i + -1
                if p.exists():
                    take_wu_and_split_h(p)
                v = i + -2
                if v.exists():
                    k = v.slot(2)
                    done(eng, s_nm, v)
                    done(eng, s_rs, v + -2)
                    eng.activation(sq[:, :], y[:, :], ACT.Square, bias=nmean[:, k:k + 1],
                                   accum_out=ssq[:, k:k + 1]).then_inc(s_sq, 1)
                if i.exists():
                    eng.wait_ge(s_hs[h], i.lap(2))
                    done(eng, s_H, i + -2)
                    for a in range(4):
                        eng.dma_start(hq[32 * a:32 * a + 32, h, :, :],
                                      htok[h, :, 128 * a:128 * a + 128].rearrange("(b j) n -> j b n", j=32))\
                           .then_inc(s_hq[h], 16)
                w = i + -3
                if w.exists():
                    store(w)
                if i.j is None and i.c == NU + 1:
                    store(i + -2)

            def store(w):
                o = eng.value_load(c_ord[0:1, bass.ds(w.value(), 1)], min_val=0, max_val=NB - 1)
                done(eng, s_o, w)
                eng.dma_start(out[bass.ds(o, 1), :, :].rearrange("a p n -> (a p) n"), ot[:, w.slot(OB), :])\
                   .then_inc(s_st[w.slot(OB)], 16)

            steps(eng, body)
            for k in range(OB):
                eng.wait_ge(s_st[k], 16 * NU // OB)

        @block.vector
        def _(eng):
            chain = [0]

            def link(ins):
                chain[0] += 1
                ins.then_inc(s_p, 1)
                eng.wait_ge(s_p, chain[0])

            eng.wait_ge(s_it, 32)
            eng.wait_ge(s_io, 2)
            link(eng.tensor_copy(rf[:, 0:NB], it_r[:, :]))
            link(eng.tensor_copy(rf[:, NB:NB + 1], it_c[:, :]))
            link(eng.tensor_copy(jf[:, 0:NB], io_r[:, :]))
            link(eng.tensor_copy(jf[:, NB:NB + 1], io_c[:, :]))
            link(eng.tensor_scalar(tf[:, :], rf[:, :], 0.0, 3.0, ALU.is_lt, ALU.mult))
            link(eng.tensor_tensor(tf[:, :], tf[:, :], rf[:, :], ALU.add))
            link(eng.tensor_scalar(rf[:, :], tf[:, :], 0.0, 2.0, ALU.max, ALU.min))
            link(eng.scalar_tensor_tensor(out=kf[:, :], in0=rf[:, :], scalar=float(NB), in1=jf[:, :],
                                          op0=ALU.mult, op1=ALU.add))
            link(eng.tensor_scalar(less[:, :], kf[:, 0:NB], kf[:, NB:NB + 1], None, ALU.is_lt))
            link(eng.reduce_sum(pos[:, :], less[:, :], mybir.AxisListType.X))
            eng.tensor_scalar(oneh[:, :], jf[:, 0:NB], pos[:, 0:1], None, ALU.is_equal).then_inc(s_oh, 1)
            eng.wait_ge(s_pc, 1)
            link(eng.tensor_copy(c_ord[:, 0:NB], pC[0:1, 0:NB]))
            link(eng.tensor_copy(c_ord[:, NB:NU], pC[0:1, 0:NB]))
            link(eng.tensor_copy(qf[:, 0:NB], pC[0:1, NB:NU]))
            link(eng.tensor_scalar(qf[:, NB:NU], pC[0:1, NB:NU], 3.0, None, ALU.add))
            link(eng.tensor_copy(c_q[:, :], qf[:, :]))
            link(eng.memset(ff[:, 0:1], 1.0))
            link(eng.tensor_tensor(ff[:, 1:NU], qf[:, 1:NU], qf[:, 0:NU - 1], ALU.not_equal))
            eng.tensor_copy(c_new[:, :], ff[:, :]).then_inc(s_ctl, 1)
            for s in (f_wd, f_wu, f_bd, f_gb):
                eng.sem_inc(s, 1)
            eng.wait_ge(s_ctl, 1)
            pd = Phases(eng, "ve_pd")
            pu = Phases(eng, "ve_pu")
            pg = Phases(eng, "ve_pg")

            def take_wd(i):
                c = pd.next()
                done(eng, s_D, i + -1)
                done(eng, s_hb, i + -1)
                eng.wait_ge(s_rbd, c * 16 + 16)
                eng.tensor_copy(cbd[:, :], rbd[:, :]).then_inc(f_bd, 1)
                for g in range(4):
                    eng.wait_ge(s_wdh, c * 4 + (g + 1))
                    s = slice(2 * g, 2 * g + 2)
                    last = eng.tensor_tensor(wdl[:, s, :], rwd[:, s, :], wdh[:, s, :].bitcast(fp32), ALU.subtract)
                last.then_inc(f_wd, 1)

            def take_wu(i):
                c = pu.next()
                done(eng, s_U, i + -1)
                for g in range(4):
                    eng.wait_ge(s_wuh, c * 4 + (g + 1))
                    s = slice(g, g + 1)
                    last = eng.tensor_tensor(wul[:, s, :], rwu[:, s, :], wuh[:, s, :].bitcast(fp32), ALU.subtract)
                last.then_inc(f_wu, 1)

            def take_gb():
                c = pg.next()
                eng.wait_ge(s_rgb, c * 32 + 32)
                eng.tensor_scalar(cgb[:, 0, :], rgb[:, 0, :], float(H) ** 0.5, None, ALU.mult)
                eng.tensor_copy(cgb[:, 1, :], rgb[:, 1, :]).then_inc(f_gb, 1)

            def transpose_x(u):
                k = u.slot(QB)
                eng.wait_ge(s_xq[k], u.lap(QB) * 4)
                done(eng, s_xl, u + -1)
                eng.transpose(xT[:, :, :, :], xq[:, k, :, :].rearrange("p b (k i) -> p k b i", i=32)).then_inc(s_T, 1)

            def split_x(u):
                if u.j is None and u.c == 0:
                    take_wd(u)
                else:
                    with eng.If(new_phase(eng, u) == 1):
                        take_wd(u)
                done(eng, s_xh, u)
                done(eng, s_D, u + -2)
                k = u.slot(2)
                eng.tensor_tensor(xl[:, k, :], xT[:, :, :, :].rearrange("p k b j -> p (k b j)"),
                                  xh[:, k, :].bitcast(fp32), ALU.subtract).then_inc(s_xl, 1)

            def body(i):
                if i.j is None and i.c == 0:
                    transpose_x(i)
                    split_x(i)
                    transpose_x(i + 1)
                if i.exists():
                    done(eng, s_D, i)
                    done(eng, s_xl, i)
                    done(eng, s_hg, i + -1)
                    eng.tensor_tensor(hb[:, :], pD[:, :], cbd[:, :], ALU.add).then_inc(s_hb, 1)
                if i.j is not None or i.c + 1 < NU:
                    split_x(i + 1)
                p = i + -1
                v = i + -2
                k = v.slot(2)
                if p.exists():
                    h = p.slot(2)
                    eng.wait_ge(s_hq[h], p.lap(2) * 4)
                    done(eng, s_hl, p + -1)
                    eng.transpose(hT[:, :, :, :], hq[:, h, :, :].rearrange("p b (k i) -> p k b i", i=32))\
                       .then_inc(s_H, 1)
                if i.j is not None or i.c + 2 < NU:
                    transpose_x(i + 2)
                if v.exists():
                    done(eng, s_U, v)
                    done(eng, s_r, v)
                    eng.scalar_tensor_tensor(out=y[:, :], in0=pU[:, :], scalar=1.0, in1=xt[:, v.slot(XB), :],
                                             op0=ALU.mult, op1=ALU.add, accum_out=ysum[:, k:k + 1]).then_inc(s_y, 1)
                    done(eng, s_y, v)
                    eng.tensor_scalar(nmean[:, k:k + 1], ysum[:, k:k + 1], -1.0 / H, None, ALU.mult)\
                       .then_inc(s_nm, 1)
                if p.exists():
                    if p.j is None and p.c == 0:
                        new = None
                        take_wu(p)
                    else:
                        new = new_phase(eng, p)
                        with eng.If(new == 1):
                            take_wu(p)
                    done(eng, s_hh, p)
                    eng.tensor_tensor(hl[:, :], hT[:, :, :, :].rearrange("p k b j -> p (k b j)"),
                                      hh[:, :].bitcast(fp32), ALU.subtract).then_inc(s_hl, 1)
                if v.exists():
                    o = v.slot(OB)
                    if (v + -OB).exists():
                        eng.wait_ge(s_st[o], (v + -OB).lap(OB))
                    done(eng, s_nm, v)
                    eng.scalar_tensor_tensor(out=ot[:, o, :], in0=y[:, :], scalar=nmean[:, k:k + 1],
                                             in1=cgb[:, 0, :], op0=ALU.add, op1=ALU.mult).then_inc(s_n, 1)
                    done(eng, s_rs, v)
                    done(eng, s_n, v)
                    eng.scalar_tensor_tensor(out=ot[:, o, :], in0=ot[:, o, :], scalar=rstd[:, k:k + 1],
                                             in1=cgb[:, 1, :], op0=ALU.mult, op1=ALU.add).then_inc(s_o, 1)
                if p.exists():
                    if p.j is None and p.c == 0:
                        take_gb()
                    else:
                        with eng.If(new == 1):
                            done(eng, s_o, p + -1)
                            take_gb()
            steps(eng, body)


_OUT = ((NB, 128, H), "float32")


def kernel(x, itok_B_1_2, L0_cond_W_down, L0_cond_b_down, L0_cond_W_up, L0_cond_b_up, L0_cond_gamma, L0_cond_beta,
           L1_cond_W_down, L1_cond_b_down, L1_cond_W_up, L1_cond_b_up, L1_cond_ln_w, L1_cond_ln_b):
    import concourse.bacc as bacc
    from concourse.bass_utils import run_bass_kernel_spmd

    given = {
        "x": x,
        "itok": itok_B_1_2,
        "Wd": np.concatenate([L0_cond_W_down, L1_cond_W_down]),
        "bd": np.concatenate([L0_cond_b_down, L1_cond_b_down]),
        "Wu": np.concatenate([L0_cond_W_up, L1_cond_W_up]),
        "bu": np.concatenate([L0_cond_b_up, L1_cond_b_up]),
        "ga": np.concatenate([L0_cond_gamma, L1_cond_ln_w]),
        "be": np.concatenate([L0_cond_beta, L1_cond_ln_b]),
    }
    nc = bacc.Bacc("TRN2", target_bir_lowering=False, num_devices=1)
    arrays, args = {}, []
    for name, a in given.items():
        a = np.ascontiguousarray(a)
        arrays[f"in_{name}"] = a
        args.append(nc.dram_tensor(f"in_{name}", a.shape, mybir.dt.from_np(a.dtype), kind="ExternalInput").ap())
    out = nc.dram_tensor("out_0", _OUT[0], mybir.dt.from_np(np.dtype(_OUT[1])), kind="ExternalOutput").ap()
    routed_adapters(nc, *args, out)
    r = run_bass_kernel_spmd(nc, [arrays], core_ids=[0])
    return r.results[0]["out_0"]
```

```python
import concourse.bass as bass
import numpy as np
from concourse import mybir
from contextlib import ExitStack

NB = 128
H = 1024
K = 512
NU = 2 * NB
XB = 4
QB = 4
OB = 2
EPS = 1e-5


class Unit:

    def __init__(self, c, j=None, m=4):
        self.c, self.j, self.m = c, j, m

    def __add__(self, d):
        return Unit(self.c + d, self.j, self.m)

    def exists(self):
        return self.j is not None or 0 <= self.c < NU

    def value(self):
        return self.c if self.j is None else self.j * self.m + self.c

    def slot(self, n):
        return self.c % n

    def lap(self, n):
        k = self.c // n + 1
        return 16 * k if self.j is None else self.j * (16 * self.m // n) + 16 * k


def routed_adapters(nc, x, itok, Wd, bd, Wu, bu, ga, be, out):
    fp32 = mybir.dt.float32
    fp32r = mybir.dt.float32r
    i32 = mybir.dt.int32
    ALU = mybir.AluOpType
    ACT = mybir.ActivationFunctionType

    ctx = ExitStack()
    with ctx:
        def sb(name, shape, dt=fp32):
            return ctx.enter_context(nc.sbuf_tensor(name, shape, dt))

        def pb(name, shape):
            return ctx.enter_context(nc.psum_tensor(name, shape, fp32))

        def sem(name):
            return ctx.enter_context(nc.semaphore(name))

        wdh = sb("wdh", [128, 8, K], fp32r)
        wdl = sb("wdl", [128, 8, K], fp32r)
        wuh = sb("wuh", [128, 4, H], fp32r)
        wul = sb("wul", [128, 4, H], fp32r)
        rwd = sb("rwd", [128, 8, K])
        rwu = sb("rwu", [128, 4, H])
        rbd = sb("rbd", [128, K])
        rbu = sb("rbu", [128, H])
        rgb = sb("rgb", [128, 2, H])
        cbd = sb("cbd", [128, K])
        cbu = sb("cbu", [128, H])
        cgb = sb("cgb", [128, 2, H])

        xt = sb("xt", [128, XB, H])
        xq = sb("xq", [128, QB, 4, 256])
        xh = sb("xh", [128, 2, H], fp32r)
        xl = sb("xl", [128, 2, H], fp32r)
        hb = sb("hb", [128, K])
        hg = sb("hg", [128, 2, K])
        hq = sb("hq", [128, 2, 4, 128])
        hh = sb("hh", [128, 2, K], fp32r)
        hl = sb("hl", [128, 2, K], fp32r)
        y = sb("y", [128, H])
        ot = sb("ot", [128, OB, H])
        ysum = sb("ysum", [128, 2])
        nmean = sb("nmean", [128, 2])
        ssq = sb("ssq", [128, 2])
        var = sb("var", [128, 2])
        rstd = sb("rstd", [128, 2])
        mhalf = sb("mhalf", [128, 1])
        htok = nc.dram_tensor("htok", [2, 128, K], fp32).ap()
        heps = sb("heps", [128, 1])
        ones = sb("ones", [128, 1])
        rooth = sb("rooth", [128, 1])

        it = sb("it", [128, NB + 1], i32)
        io = sb("io", [128, NB + 1], i32)
        rf, tf, kf = (ot[:, 0, (NB + 1) * n:(NB + 1) * (n + 1)] for n in range(3))
        less, oneh = (ot[:, 1, NB * n:NB * (n + 1)] for n in range(2))
        jf = sb("jf", [128, 1])
        pos = sb("pos", [128, 1])
        c_ord = sb("c_ord", [1, NU], i32)
        c_q = sb("c_q", [1, NU], i32)
        c_new = sb("c_new", [1, NU], i32)

        pD = pb("pD", [128, K])
        pU = pb("pU", [128, H])
        sq = pb("sq", [128, H])
        xT = pb("xT", [128, H])
        hT = pb("hT", [128, K])
        pC = hT

        s_it = sem("s_it")
        s_io = sem("s_io")
        s_id = sem("s_id")
        s_p = sem("s_p")
        s_oh = sem("s_oh")
        s_pc = sem("s_pc")
        s_ctl = sem("s_ctl")
        s_rd = [sem(f"s_rd{g}") for g in range(2)]
        s_ru = [sem(f"s_ru{g}") for g in range(2)]
        s_rbd = sem("s_rbd")
        s_rbu = sem("s_rbu")
        s_rgb = sem("s_rgb")
        f_wd = sem("f_wd")
        f_wu = sem("f_wu")
        f_bd = sem("f_bd")
        f_gb = sem("f_gb")
        f_bu = sem("f_bu")
        s_wdh = sem("s_wdh")
        s_wd = sem("s_wd")
        s_wu = sem("s_wu")
        s_wuh = sem("s_wuh")
        s_x = [sem(f"s_x{k}") for k in range(XB)]
        s_st = [sem(f"s_st{k}") for k in range(OB)]
        s_r = sem("s_r")
        s_cb = sem("s_cb")
        s_xq = [sem(f"s_xq{k}") for k in range(QB)]
        s_T = sem("s_T")
        s_D = sem("s_D")
        s_U = sem("s_U")
        s_hs = [sem(f"s_hs{k}") for k in range(2)]
        s_hq = [sem(f"s_hq{k}") for k in range(2)]
        s_H = sem("s_H")
        s_xh = sem("s_xh")
        s_xl = sem("s_xl")
        s_hb = sem("s_hb")
        s_hg = sem("s_hg")
        s_hh = sem("s_hh")
        s_hl = sem("s_hl")
        s_y = sem("s_y")
        s_nm = sem("s_nm")
        s_sq = sem("s_sq")
        s_var = sem("s_var")
        s_rs = sem("s_rs")
        s_n = sem("s_n")
        s_o = sem("s_o")
        s_cd = sem("s_cd")
        s_cg = sem("s_cg")

        def done(eng, s, u):
            if u.exists():
                eng.wait_ge(s, u.value() + 1)

        def quarter(eng, s, u, g):
            eng.wait_ge(s, 4 * u.c + g + 1 if u.j is None else u.j * (4 * u.m) + (4 * u.c + g + 1))

        def up_part(g):
            return slice(2 * (g % 2), 2 * (g % 2) + 2), slice(K * (g // 2), K * (g // 2) + K)

        def steps(eng, body):
            for c in range(4):
                body(Unit(c))
            with eng.Fori(0, NU // 4 - 2) as j:
                for m in range(4):
                    body(Unit(4 + m, j))
            for c in range(NU - 4, NU + 2):
                body(Unit(c))

        def new_phase(eng, u):
            return eng.value_load(c_new[0:1, bass.ds(u.value(), 1)], min_val=0, max_val=1)

        class Phases:

            def __init__(self, eng, name):
                self.eng = eng
                self.reg = eng.alloc_register(name)
                eng.reg_mov(self.reg, 0)

            def next(self):
                before = self.eng.snap(self.reg)
                self.eng.reg_add(self.reg, self.reg, 1)
                return before

        block = ctx.enter_context(nc.Block())

        @block.sync
        def _(eng):
            eng.dma_start(it[:, 0:NB], itok.rearrange("(a n) -> a n", a=1).broadcast_to([128, NB])).then_inc(s_it, 16)
            eng.dma_start(it[:, NB:NB + 1], itok.rearrange("(n a) -> n a", a=1)).then_inc(s_it, 16)
            eng.wait_ge(s_ctl, 1)
            pd = Phases(eng, "sp_pd")
            pu = Phases(eng, "sp_pu")

            def load_down(u):
                q = eng.value_load(c_q[0:1, bass.ds(u.value(), 1)], min_val=0, max_val=5)
                c = pd.next()
                row = bass.ds(q, 1)
                eng.wait_ge(f_wd, c + 1)
                for g in range(2):
                    for a in range(4):
                        eng.dma_start(rwd[32 * a:32 * a + 32, 4 * g:4 * g + 4, :],
                                      Wd[row, 256 * a + 128 * g:256 * a + 128 * g + 128, :]
                                      .rearrange("a (k i) n -> (a i) k n", i=32)).then_inc(s_rd[g], 16)
                eng.wait_ge(f_bd, c + 1)
                eng.dma_start(rbd[:, :], bd[row, :].broadcast_to([128, K])).then_inc(s_rbd, 16)
                eng.wait_ge(f_bu, c + 1)
                eng.dma_start(rbu[:, :], bu[row, :].broadcast_to([128, H])).then_inc(s_rbu, 16)

            def load_up(u):
                q = eng.value_load(c_q[0:1, bass.ds(u.value(), 1)], min_val=0, max_val=5)
                c = pu.next()
                row = bass.ds(q, 1)
                eng.wait_ge(f_wu, c + 1)
                for g in range(2):
                    for a in range(4):
                        eng.dma_start(rwu[32 * a:32 * a + 32, 2 * g:2 * g + 2, :],
                                      Wu[row, 128 * a + 64 * g:128 * a + 64 * g + 64, :]
                                      .rearrange("a (k i) n -> (a i) k n", i=32)).then_inc(s_ru[g], 16)
                eng.wait_ge(f_gb, c + 1)
                eng.dma_start(rgb[:, 0, :], ga[row, :].broadcast_to([128, H])).then_inc(s_rgb, 16)
                eng.dma_start(rgb[:, 1, :], be[row, :].broadcast_to([128, H])).then_inc(s_rgb, 16)

            def load_q(u, src):
                o = eng.value_load(c_ord[0:1, bass.ds(u.value(), 1)], min_val=0, max_val=NB - 1)
                k = u.slot(QB)
                done(eng, s_T, u + -QB)
                for a in range(4):
                    eng.dma_start(xq[32 * a:32 * a + 32, k, :, :],
                                  src[bass.ds(o, 1), :, 256 * a:256 * a + 256]
                                  .rearrange("a (b j) n -> (a j) b n", j=32)).then_inc(s_xq[k], 16)

            def load_t(u, src):
                o = eng.value_load(c_ord[0:1, bass.ds(u.value(), 1)], min_val=0, max_val=NB - 1)
                k = u.slot(XB)
                done(eng, s_y, u + -XB)
                eng.dma_start(xt[:, k, :], src[bass.ds(o, 1), :, :].rearrange("a p n -> (a p) n"))\
                   .then_inc(s_x[k], 16)

            def maybe_up(u):
                if u.j is None and u.c == 0:
                    load_up(u)
                elif u.exists():
                    with eng.If(new_phase(eng, u) == 1):
                        load_up(u)

            def load(u, src, before):
                t = u + -2
                load_q(u, src)
                if t.exists():
                    load_t(t, before)
                if u.j is None and u.c == 0:
                    load_down(u)
                else:
                    with eng.If(new_phase(eng, u) == 1):
                        load_down(u)
                maybe_up(u + -2)

            for c in range(8):
                load(Unit(c), x, x)
            with eng.Fori(0, NB // 4 - 2) as j:
                for m in range(4):
                    load(Unit(8 + m, j), x, x)
            for c in range(NB, NB + 4):
                eng.wait_ge(s_st[c % OB], Unit(c - NB).lap(OB))
                load(Unit(c), out, x if c < NB + 2 else out)
            with eng.Fori(0, NB // 4 - 1) as j:
                for m in range(4):
                    eng.wait_ge(s_st[m % OB], Unit(4 + m, j).lap(OB))
                    load(Unit(NB + 4 + m, j), out, out)
            for c in range(NU - 2, NU):
                load_t(Unit(c), out)
                maybe_up(Unit(c))

        @block.gpsimd
        def _(eng):
            eng.iota(io[:, 0:NB], pattern=[[1, NB]], base=0, channel_multiplier=0).then_inc(s_io, 1)
            eng.iota(io[:, NB:NB + 1], pattern=[[1, 1]], base=0, channel_multiplier=1).then_inc(s_io, 1)
            eng.memset(mhalf[:, :], -0.5).then_inc(s_id, 1)
            eng.memset(heps[:, :], H * EPS).then_inc(s_id, 1)
            eng.memset(ones[:, :], 1.0).then_inc(s_id, 1)
            eng.memset(rooth[:, :], float(H) ** 0.5).then_inc(s_id, 1)
            eng.wait_ge(s_id, 4)
            for s in (f_bu, f_gb):
                eng.sem_inc(s, 1)
            eng.wait_ge(s_ctl, 1)
            phases = Phases(eng, "pl_ph")
            pg = Phases(eng, "pl_pg")

            def take_gb(p):
                if p.exists():
                    if p.j is None and p.c == 0:
                        copy_gb(p, pg.next())
                    else:
                        with eng.If(new_phase(eng, p) == 1):
                            copy_gb(p, pg.next())
                    eng.drain().then_inc(s_cg, 1)

            def copy_gb(p, c):
                done(eng, s_o, p + -1)
                eng.wait_ge(s_rgb, c * 32 + 32)
                eng.tensor_tensor(cgb[:, 0, :], rgb[:, 0, :], rooth[:, 0:1].broadcast_to([128, H]), ALU.mult)
                eng.tensor_tensor(cgb[:, 1, :], rgb[:, 1, :], ones[:, 0:1].broadcast_to([128, H]), ALU.mult)\
                   .then_inc(f_gb, 1)

            def take_bu(u, c):
                done(eng, s_r, u + -1)
                eng.wait_ge(s_rbu, c * 16 + 16)
                eng.tensor_tensor(cbu[:, :], rbu[:, :], ones[:, 0:1].broadcast_to([128, H]), ALU.mult).then_inc(f_bu, 1)

            def residual(u):
                if u.j is None and u.c == 0:
                    take_bu(u, phases.next())
                else:
                    with eng.If(new_phase(eng, u) == 1):
                        take_bu(u, phases.next())
                eng.drain().then_inc(s_cb, 1)
                done(eng, s_cb, u)
                eng.wait_ge(s_x[u.slot(XB)], u.lap(XB))
                done(eng, s_hb, u)
                eng.tensor_tensor(xt[:, u.slot(XB), :], xt[:, u.slot(XB), :], cbu[:, :], ALU.add).then_inc(s_r, 1)

            def body(i):
                if i.exists():
                    residual(i)
                v = i + -2
                if v.exists():
                    k = v.slot(2)
                    done(eng, s_sq, v)
                    eng.tensor_tensor(var[:, k:k + 1], ssq[:, k:k + 1], heps[:, :], ALU.add).then_inc(s_var, 1)
                    done(eng, s_var, v)
                    eng.tensor_tensor(rstd[:, k:k + 1], var[:, k:k + 1], mhalf[:, :], ALU.pow).then_inc(s_rs, 1)
                take_gb(i + -1)

            steps(eng, body)

        @block.tensor
        def _(eng):
            eng.wait_ge(s_oh, 2)
            eng.matmul(pC[0:1, 0:NB], jf[:, :], oneh[:, :], start=True, stop=True)
            eng.matmul(pC[0:1, NB:NU], rf[:, NB:NB + 1], oneh[:, :], start=True, stop=True).then_inc(s_pc, 1)

            def body(i):
                if i.exists():
                    done(eng, s_xh, i)
                    done(eng, s_xl, i)
                    done(eng, s_hb, i + -1)
                    n = 0
                    b = i.slot(2)
                    for k in range(8):
                        if k % 2 == 0:
                            quarter(eng, s_wd, i, k // 2)
                        for a, w in ((xh, wdh), (xh, wdl), (xl, wdh)):
                            last = eng.matmul(pD[:, :], a[:, b, 128 * k:128 * k + 128], w[:, k, :],
                                              start=(n == 0), stop=(n == 23))
                            n += 1
                    last.then_inc(s_D, 1)
                v = i + -2
                if v.exists():
                    done(eng, s_hh, v)
                    done(eng, s_hl, v)
                    done(eng, s_y, v + -1)
                    for m in range(2):
                        n = 0
                        for k in range(4):
                            if k % 2 == 0:
                                quarter(eng, s_wu, v, 2 * m + k // 2)
                            for a, w in ((hh, wuh), (hh, wul), (hl, wuh)):
                                last = eng.matmul(pU[:, K * m:K * m + K], a[:, v.slot(2), 128 * k:128 * k + 128],
                                                  w[:, k, K * m:K * m + K], start=(n == 0), stop=(n == 11))
                                n += 1
                    last.then_inc(s_U, 1)

            steps(eng, body)

        @block.scalar
        def _(eng):
            eng.wait_ge(s_ctl, 1)
            pd = Phases(eng, "ac_pd")
            pu = Phases(eng, "ac_pu")

            def take_wd(i):
                c = pd.next()
                done(eng, s_D, i + -1)
                for g in range(4):
                    eng.wait_ge(s_rd[g // 2], c * 64 + 64)
                    eng.activation(wdh[:, 2 * g:2 * g + 2, :], rwd[:, 2 * g:2 * g + 2, :], ACT.Copy)\
                       .then_inc(s_wdh, 1)

            def take_wu(i):
                c = pu.next()
                done(eng, s_U, i + -1)
                for g in range(4):
                    kk, nn = up_part(g)
                    eng.wait_ge(s_ru[g % 2], c * 64 + 64)
                    eng.activation(wuh[:, kk, nn], rwu[:, kk, nn], ACT.Copy).then_inc(s_wuh, 1)

            def split_x(u):
                done(eng, s_T, u)
                done(eng, s_D, u + -2)
                eng.activation(xh[:, u.slot(2), :], xT[:, :], ACT.Copy).then_inc(s_xh, 1)
                if u.j is None and u.c == 0:
                    take_wd(u)
                else:
                    with eng.If(new_phase(eng, u) == 1):
                        take_wd(u)

            def split_h(p):
                done(eng, s_H, p)
                done(eng, s_U, p + -2)
                eng.activation(hh[:, p.slot(2), :], hT[:, :], ACT.Copy)\
                   .then_inc(s_hh, 1)

            def body(i):
                if i.j is None and i.c == 0:
                    split_x(i)
                if i.j is not None or i.c + 1 < NU:
                    split_x(i + 1)
                h = i.slot(2)
                if i.exists():
                    done(eng, s_hb, i)
                    if (i + -2).exists():
                        eng.wait_ge(s_hs[h], (i + -2).lap(2))
                    eng.activation(hg[:, h, :], hb[:, :], ACT.Gelu).then_inc(s_hg, 1)
                    if (i + -2).exists():
                        eng.wait_ge(s_hq[h], (i + -2).lap(2) * 4)
                    done(eng, s_hg, i)
                    eng.dma_start(htok[h, :, :], hg[:, h, :]).then_inc(s_hs[h], 16)
                p = i + -1
                last = i.j is None and i.c == NU - 1
                if p.exists():
                    split_h(p)
                if last:
                    load_h(i)
                v = i + -2
                if v.exists():
                    k = v.slot(2)
                    done(eng, s_nm, v)
                    done(eng, s_rs, v + -2)
                    eng.activation(sq[:, :], y[:, :], ACT.Square, bias=nmean[:, k:k + 1],
                                   accum_out=ssq[:, k:k + 1]).then_inc(s_sq, 1)
                if p.j is None and p.c == 0:
                    take_wu(p)
                elif p.exists():
                    with eng.If(new_phase(eng, p) == 1):
                        take_wu(p)
                if i.exists() and not last:
                    load_h(i)
                w = i + -3
                if w.exists():
                    store(w)
                if i.j is None and i.c == NU + 1:
                    store(i + -2)

            def load_h(i):
                h = i.slot(2)
                eng.wait_ge(s_hs[h], i.lap(2))
                done(eng, s_H, i + -2)
                for a in range(4):
                    eng.dma_start(hq[32 * a:32 * a + 32, h, :, :],
                                  htok[h, :, 128 * a:128 * a + 128].rearrange("(b j) n -> j b n", j=32))\
                       .then_inc(s_hq[h], 16)

            def store(w):
                o = eng.value_load(c_ord[0:1, bass.ds(w.value(), 1)], min_val=0, max_val=NB - 1)
                done(eng, s_o, w)
                eng.dma_start(out[bass.ds(o, 1), :, :].rearrange("a p n -> (a p) n"), ot[:, w.slot(OB), :])\
                   .then_inc(s_st[w.slot(OB)], 16)

            steps(eng, body)
            for k in range(OB):
                eng.wait_ge(s_st[k], 16 * NU // OB)

        @block.vector
        def _(eng):
            chain = [0]

            def link(ins):
                chain[0] += 1
                ins.then_inc(s_p, 1)
                eng.wait_ge(s_p, chain[0])

            eng.wait_ge(s_it, 32)
            eng.wait_ge(s_io, 2)
            eng.tensor_copy(jf[:, :], io[:, NB:NB + 1]).then_inc(s_oh, 1)
            link(eng.tensor_scalar(tf[:, :], it[:, :], 0.0, 3.0, ALU.is_lt, ALU.mult))
            link(eng.tensor_tensor(tf[:, :], tf[:, :], it[:, :], ALU.add))
            link(eng.tensor_scalar(rf[:, :], tf[:, :], 0.0, 2.0, ALU.max, ALU.min))
            link(eng.scalar_tensor_tensor(out=kf[:, :], in0=rf[:, :], scalar=float(NB), in1=io[:, :],
                                          op0=ALU.mult, op1=ALU.add))
            link(eng.tensor_scalar(less[:, :], kf[:, 0:NB], kf[:, NB:NB + 1], None, ALU.is_lt))
            link(eng.reduce_sum(pos[:, :], less[:, :], mybir.AxisListType.X))
            eng.tensor_scalar(oneh[:, :], io[:, 0:NB], pos[:, 0:1], None, ALU.is_equal).then_inc(s_oh, 1)
            eng.wait_ge(s_pc, 1)
            eng.tensor_copy(c_ord[:, 0:NB], pC[0:1, 0:NB])
            eng.tensor_copy(c_ord[:, NB:NU], pC[0:1, 0:NB])
            eng.tensor_copy(c_q[:, 0:NB], pC[0:1, NB:NU])
            eng.memset(c_new[:, 0:1], 1)
            link(eng.tensor_scalar(c_q[:, NB:NU], pC[0:1, NB:NU], 3.0, None, ALU.add))
            eng.tensor_tensor(c_new[:, 1:NU], c_q[:, 1:NU], c_q[:, 0:NU - 1], ALU.not_equal).then_inc(s_ctl, 1)
            for s in (f_wd, f_wu, f_bd):
                eng.sem_inc(s, 1)
            eng.wait_ge(s_ctl, 1)
            pd = Phases(eng, "ve_pd")
            pu = Phases(eng, "ve_pu")

            def take_wd(i):
                c = pd.next()
                done(eng, s_D, i + -1)
                for g in range(4):
                    eng.wait_ge(s_wdh, c * 4 + (g + 1))
                    s = slice(2 * g, 2 * g + 2)
                    eng.tensor_tensor(wdl[:, s, :], rwd[:, s, :], wdh[:, s, :].bitcast(fp32), ALU.subtract)\
                       .then_inc(s_wd, 1)
                done(eng, s_hb, i + -1)
                eng.wait_ge(s_rbd, c * 16 + 16)
                eng.tensor_copy(cbd[:, :], rbd[:, :]).then_inc(f_bd, 1)
                quarter(eng, s_wd, i, 3)
                eng.sem_inc(f_wd, 1)

            def take_wu(i):
                c = pu.next()
                done(eng, s_U, i + -1)
                for g in range(4):
                    eng.wait_ge(s_wuh, c * 4 + (g + 1))
                    kk, nn = up_part(g)
                    eng.tensor_tensor(wul[:, kk, nn], rwu[:, kk, nn], wuh[:, kk, nn].bitcast(fp32), ALU.subtract)\
                       .then_inc(s_wu, 1)
                quarter(eng, s_wu, i, 3)
                eng.sem_inc(f_wu, 1)

            def transpose_x(u):
                k = u.slot(QB)
                eng.wait_ge(s_xq[k], u.lap(QB) * 4)
                done(eng, s_xl, u + -1)
                eng.transpose(xT[:, :].rearrange("p (k b j) -> p k b j", b=4, j=32), xq[:, k, :, :].rearrange("p b (k i) -> p k b i", i=32)).then_inc(s_T, 1)

            def split_x(u):
                done(eng, s_xh, u)
                done(eng, s_D, u + -2)
                k = u.slot(2)
                eng.tensor_tensor(xl[:, k, :], xT[:, :],
                                  xh[:, k, :].bitcast(fp32), ALU.subtract).then_inc(s_xl, 1)
                if u.j is None and u.c == 0:
                    take_wd(u)
                else:
                    new = new_phase(eng, u)
                    with eng.If(new == 1):
                        take_wd(u)
                    with eng.If(new == 0):
                        eng.sem_inc(s_wd, 4)

            def low_h(p):
                h = p.slot(2)
                done(eng, s_hh, p)
                done(eng, s_U, p + -2)
                eng.tensor_tensor(hl[:, h, :], hT[:, :],
                                  hh[:, h, :].bitcast(fp32), ALU.subtract).then_inc(s_hl, 1)

            def old_wu(p, new):
                with eng.If(new == 0):
                    eng.sem_inc(s_wu, 4)

            def body(i):
                if i.j is None and i.c == 0:
                    transpose_x(i)
                    split_x(i)
                    transpose_x(i + 1)
                if i.exists():
                    done(eng, s_D, i)
                    if i.j is None and i.c == 0:
                        eng.wait_ge(f_bd, 2)
                    if i.j is not None or i.c + 1 < NU:
                        done(eng, s_T, i + 1)
                    done(eng, s_hg, i + -1)
                    eng.tensor_tensor(hb[:, :], pD[:, :], cbd[:, :], ALU.add).then_inc(s_hb, 1)
                if i.j is not None or i.c + 1 < NU:
                    split_x(i + 1)
                p = i + -1
                v = i + -2
                k = v.slot(2)
                if p.exists():
                    h = p.slot(2)
                    eng.wait_ge(s_hq[h], p.lap(2) * 4)
                    done(eng, s_hl, p + -1)
                    eng.transpose(hT[:, :].rearrange("p (k b j) -> p k b j", b=4, j=32), hq[:, h, :, :].rearrange("p b (k i) -> p k b i", i=32))\
                       .then_inc(s_H, 1)
                if i.j is not None or i.c + 2 < NU:
                    transpose_x(i + 2)
                end = i.j is None and i.c >= NU - 1
                if end and p.exists():
                    low_h(p)
                    old_wu(p, new_phase(eng, p))
                if v.exists():
                    done(eng, s_U, v)
                    done(eng, s_r, v)
                    eng.scalar_tensor_tensor(out=y[:, :], in0=pU[:, :], scalar=1.0, in1=xt[:, v.slot(XB), :],
                                             op0=ALU.mult, op1=ALU.add, accum_out=ysum[:, k:k + 1]).then_inc(s_y, 1)
                    done(eng, s_y, v)
                    eng.tensor_scalar(nmean[:, k:k + 1], ysum[:, k:k + 1], -1.0 / H, None, ALU.mult)\
                       .then_inc(s_nm, 1)
                if p.exists() and not end:
                    low_h(p)
                if v.exists():
                    o = v.slot(OB)
                    if (v + -OB).exists():
                        eng.wait_ge(s_st[o], (v + -OB).lap(OB))
                    done(eng, s_nm, v)
                    done(eng, s_cg, v)
                    eng.scalar_tensor_tensor(out=ot[:, o, :], in0=y[:, :], scalar=nmean[:, k:k + 1],
                                             in1=cgb[:, 0, :], op0=ALU.add, op1=ALU.mult).then_inc(s_n, 1)
                if p.exists():
                    if p.j is None and p.c == 0:
                        take_wu(p)
                    else:
                        new = new_phase(eng, p)
                        with eng.If(new == 1):
                            take_wu(p)
                        if not end:
                            old_wu(p, new)
                if v.exists():
                    o = v.slot(OB)
                    done(eng, s_rs, v)
                    done(eng, s_n, v)
                    eng.scalar_tensor_tensor(out=ot[:, o, :], in0=ot[:, o, :], scalar=rstd[:, k:k + 1],
                                             in1=cgb[:, 1, :], op0=ALU.mult, op1=ALU.add).then_inc(s_o, 1)
            steps(eng, body)


_OUT = ((NB, 128, H), "float32")


def kernel(x, itok_B_1_2, L0_cond_W_down, L0_cond_b_down, L0_cond_W_up, L0_cond_b_up, L0_cond_gamma, L0_cond_beta,
           L1_cond_W_down, L1_cond_b_down, L1_cond_W_up, L1_cond_b_up, L1_cond_ln_w, L1_cond_ln_b):
    import concourse.bacc as bacc
    from concourse.bass_utils import run_bass_kernel_spmd

    given = {
        "x": x,
        "itok": itok_B_1_2,
        "Wd": np.concatenate([L0_cond_W_down, L1_cond_W_down]),
        "bd": np.concatenate([L0_cond_b_down, L1_cond_b_down]),
        "Wu": np.concatenate([L0_cond_W_up, L1_cond_W_up]),
        "bu": np.concatenate([L0_cond_b_up, L1_cond_b_up]),
        "ga": np.concatenate([L0_cond_gamma, L1_cond_ln_w]),
        "be": np.concatenate([L0_cond_beta, L1_cond_ln_b]),
    }
    nc = bacc.Bacc("TRN2", target_bir_lowering=False, num_devices=1)
    arrays, args = {}, []
    for name, a in given.items():
        a = np.ascontiguousarray(a)
        arrays[f"in_{name}"] = a
        args.append(nc.dram_tensor(f"in_{name}", a.shape, mybir.dt.from_np(a.dtype), kind="ExternalInput").ap())
    out = nc.dram_tensor("out_0", _OUT[0], mybir.dt.from_np(np.dtype(_OUT[1])), kind="ExternalOutput").ap()
    routed_adapters(nc, *args, out)
    r = run_bass_kernel_spmd(nc, [arrays], core_ids=[0])
    return r.results[0]["out_0"]
```
